# Optimizing a Trainium2 kernel written in Bass

```python
import numpy as np
import jax
import jax.numpy as jnp

def _softmax(x, axis=-1):
    return jax.nn.softmax(x, axis=axis)

def _gelu(x):
    return jax.nn.gelu(x, approximate=True)

def _silu(x):
    return jax.nn.silu(x)

def _sigmoid(x):
    return jax.nn.sigmoid(x)

def _layernorm(x, axis=-1, eps=1e-05):
    m = jnp.mean(x, axis=axis, keepdims=True)
    v = jnp.var(x, axis=axis, keepdims=True)
    return (x - m) / jnp.sqrt(v + eps)

def _scatter_add(tgt, idx, src, axis=0):
    return tgt.at[idx].add(src)

def _segment_sum(src, seg, n):
    return jax.ops.segment_sum(src, seg, n)
kernel_name = 'mk_adaln_ffn_d1_seqx_r2_428bd9'

def setup_inputs(seed: int=0):
    np.random.seed(seed)
    _w = jnp.asarray

    def _rec_inputs():
        import jax
        import jax.numpy as jnp
        _rk = jax.random.key(seed)
        x = -0.000125 + 0.9999 * jax.random.normal(jax.random.fold_in(_rk, 1), (32, 128, 2048), jnp.float32)
        _lenS = 128 - jax.random.randint(jax.random.fold_in(_rk, 7), (32,), 0, max(1, 128 // 4) + 1, jnp.int32)
        _lenS2 = 128 - jax.random.randint(jax.random.fold_in(_rk, 8), (32,), 0, max(1, 128 // 4) + 1, jnp.int32)
        cond_128 = 0.0061147 + 1.02565 * jax.random.normal(jax.random.fold_in(_rk, 11), (32, 128), jnp.float32)
        return (x, cond_128)
    x, cond_128 = _rec_inputs()

    def _L0_cond_setup():
        import jax, jax.numpy as jnp
        import numpy as np
        K = 8
        T = 1.0
        D_EMBD = 128
        IN_C = 128
        OUT_C = 128
        BS = 32
        H = 2048
        HID = 128
        key = jax.random.key(seed)
        ks = jax.random.split(key, 10)
        s = lambda fan_in: 1.0 / np.sqrt(fan_in)
        return {'x': jax.random.normal(ks[0], (BS, IN_C, H), dtype=jnp.float32), 'embedding': jax.random.normal(ks[1], (BS, D_EMBD), dtype=jnp.float32), 'W0': jax.random.normal(ks[2], (D_EMBD, HID), dtype=jnp.float32) * s(D_EMBD), 'b0': jnp.zeros((HID,), dtype=jnp.float32), 'W1': jax.random.normal(ks[3], (HID, HID), dtype=jnp.float32) * s(HID), 'b1': jnp.zeros((HID,), dtype=jnp.float32), 'W2': jax.random.normal(ks[4], (HID, K), dtype=jnp.float32) * s(HID), 'b2': jnp.zeros((K,), dtype=jnp.float32), 'weight': jax.random.normal(ks[5], (K, OUT_C, IN_C, 1), dtype=jnp.float32) * s(IN_C), 'bias_k': jax.random.normal(ks[6], (K, OUT_C), dtype=jnp.float32) * 0.1}
    _L0_cond_all = _L0_cond_setup()
    _L0_cond_in = {k: v for k, v in _L0_cond_all.items() if k in ('W0', 'b0', 'W1', 'b1', 'W2', 'b2', 'weight', 'bias_k')}
    del _L0_cond_all

    def _L0_ffn_setup():
        import jax, jax.numpy as jnp
        import numpy as np

        def sparsemax(z):
            E = z.shape[-1]
            z_sorted = -jnp.sort(-z, axis=-1)
            z_cum = jnp.cumsum(z_sorted, axis=-1)
            k = jnp.arange(1, E + 1, dtype=z.dtype)
            support = 1.0 + k * z_sorted > z_cum
            k_z = jnp.sum(support, axis=-1, keepdims=True)
            tau_sum = jnp.take_along_axis(z_cum, k_z.astype(jnp.int32) - 1, axis=-1)
            tau = (tau_sum - 1.0) / k_z.astype(z.dtype)
            return jnp.maximum(z - tau, 0.0)
        key = jax.random.key(seed)
        ks = jax.random.split(key, 6)
        B, S, D_IN, D_OUT, E, R = (8, 1024, 2048, 2048, 8, 16)
        x = jax.random.normal(ks[0], (B, S, D_IN), dtype=jnp.float32)
        W_base = jax.random.normal(ks[1], (D_OUT, D_IN), dtype=jnp.float32) * D_IN ** (-0.5)
        b_base = jax.random.normal(ks[2], (D_OUT,), dtype=jnp.float32) * 0.01
        W_router = jax.random.normal(ks[3], (E, D_IN), dtype=jnp.float32) * D_IN ** (-0.5)
        b_router = jnp.zeros((E,), dtype=jnp.float32)
        lora_A = jax.random.normal(ks[4], (E, D_IN, R), dtype=jnp.float32) * D_IN ** (-0.5)
        lora_B = jnp.zeros((E, R, D_OUT), dtype=jnp.float32)
        return {'x': x, 'W_base': W_base, 'b_base': b_base, 'W_router': W_router, 'b_router': b_router, 'lora_A': lora_A, 'lora_B': lora_B}
    _L0_ffn_all = _L0_ffn_setup()
    _L0_ffn_in = {k: v for k, v in _L0_ffn_all.items() if k in ('W_base', 'b_base', 'W_router', 'b_router', 'lora_A', 'lora_B')}
    del _L0_ffn_all
    return {'x': x, 'cond_128': cond_128, 'L0_cond_W0': _L0_cond_in['W0'], 'L0_cond_b0': _L0_cond_in['b0'], 'L0_cond_W1': _L0_cond_in['W1'], 'L0_cond_b1': _L0_cond_in['b1'], 'L0_cond_W2': _L0_cond_in['W2'], 'L0_cond_b2': _L0_cond_in['b2'], 'L0_cond_weight': _L0_cond_in['weight'], 'L0_cond_bias_k': _L0_cond_in['bias_k'], 'L0_ffn_W_base': _L0_ffn_in['W_base'], 'L0_ffn_b_base': _L0_ffn_in['b_base'], 'L0_ffn_W_router': _L0_ffn_in['W_router'], 'L0_ffn_b_router': _L0_ffn_in['b_router'], 'L0_ffn_lora_A': _L0_ffn_in['lora_A'], 'L0_ffn_lora_B': _L0_ffn_in['lora_B']}

def reference(x, cond_128, L0_cond_W0, L0_cond_b0, L0_cond_W1, L0_cond_b1, L0_cond_W2, L0_cond_b2, L0_cond_weight, L0_cond_bias_k, L0_ffn_W_base, L0_ffn_b_base, L0_ffn_W_router, L0_ffn_b_router, L0_ffn_lora_A, L0_ffn_lora_B):
    import jax
    import jax.numpy as jnp

    def _L0_cond_ref(x, embedding, W0, b0, W1, b1, W2, b2, weight, bias_k):
        import jax, jax.numpy as jnp
        import numpy as np
        K = 8
        T = 1.0
        D_EMBD = 128
        IN_C = 128
        OUT_C = 128
        BS = 32
        H = 2048
        HID = 128
        h = jax.nn.gelu(embedding @ W0 + b0, approximate=False)
        h = jax.nn.gelu(h @ W1 + b1, approximate=False)
        att = jax.nn.softmax((h @ W2 + b2) / T, axis=-1)
        agg_w = jnp.einsum('bk,koi->boi', att, weight[..., 0])
        agg_b = att @ bias_k
        out = jnp.einsum('boi,bih->boh', agg_w, x) + agg_b[:, :, None]
        return out

    def _L0_ffn_ref(x, W_base, b_base, W_router, b_router, lora_A, lora_B):
        import jax, jax.numpy as jnp
        import numpy as np

        def sparsemax(z):
            E = z.shape[-1]
            z_sorted = -jnp.sort(-z, axis=-1)
            z_cum = jnp.cumsum(z_sorted, axis=-1)
            k = jnp.arange(1, E + 1, dtype=z.dtype)
            support = 1.0 + k * z_sorted > z_cum
            k_z = jnp.sum(support, axis=-1, keepdims=True)
            tau_sum = jnp.take_along_axis(z_cum, k_z.astype(jnp.int32) - 1, axis=-1)
            tau = (tau_sum - 1.0) / k_z.astype(z.dtype)
            return jnp.maximum(z - tau, 0.0)
        base_out = jnp.einsum('bsd,od->bso', x, W_base) + b_base
        logits = jnp.einsum('bsd,ed->bse', x, W_router) + b_router
        weights = sparsemax(logits)
        h = jnp.einsum('bsd,edr->bser', x, lora_A)
        expert_out = jnp.einsum('bser,bse,ero->bso', h, weights, lora_B)
        return base_out + expert_out
    x = x + _L0_ffn_ref(_L0_cond_ref(x, cond_128, L0_cond_W0, L0_cond_b0, L0_cond_W1, L0_cond_b1, L0_cond_W2, L0_cond_b2, L0_cond_weight, L0_cond_bias_k), L0_ffn_W_base, L0_ffn_b_base, L0_ffn_W_router, L0_ffn_b_router, L0_ffn_lora_A, L0_ffn_lora_B)
    return x

_drawn_inputs = setup_inputs


def setup_inputs(seed=0):
    import zlib

    import numpy as np

    out = dict(_drawn_inputs(seed))
    spreads = {'L0_cond_b0': (0.0, 0.497),
     'L0_cond_b1': (0.0, 0.31),
     'L0_cond_b2': (0.0, 0.282),
     'L0_ffn_b_router': (0.0, 0.676),
     'L0_ffn_lora_B': (0.0, 0.1)}
    factors = {'L0_ffn_b_base': 6.102}
    for name, (base, spread) in spreads.items():
        noise = np.random.default_rng([zlib.crc32(name.encode()), seed]).standard_normal(out[name].shape)
        drawn = base * np.exp(spread * noise) if base else spread * noise
        out[name] = jnp.asarray(drawn.astype(out[name].dtype))
    for name, factor in factors.items():
        out[name] = (out[name] * factor).astype(out[name].dtype)
    return out
```

```python
import concourse.bass as bass
from concourse import mybir
from contextlib import ExitStack

F32 = mybir.dt.float32
F32R = mybir.dt.float32r
ALU = mybir.AluOpType
ACT = mybir.ActivationFunctionType
AX = mybir.AxisListType

BATCH = 32
CH = 128
HID = 2048
DOUT = 2048
EXP = 8
RANK = 16
KERN = 8
P = 128

ER = EXP * RANK
RT = ER + EXP
HALVES = 2
BANK = 512
BANKS = DOUT // HALVES // BANK
CHUNKS = HID // P
CPP = 2
PIECES = CHUNKS // CPP
PW = CPP * CH
XSLOTS = 4
RAW = 4
RT_CH = 4
AHEAD = 3
STEPS = HALVES * BATCH
NPIECES = STEPS * PIECES


def arrival_order():
    order = []
    for i in range(PIECES):
        order.append(("x", i))
        if i % (RT_CH // CPP) == 0:
            order.append(("rt", i * CPP // RT_CH))
        order += [("w", 0, c, j) for c in range(CPP * i, CPP * i + CPP) for j in range(BANKS)]
    order += [("x", PIECES + i) for i in range(AHEAD)]
    order += [("b", 0, j) for j in range(BANKS)]
    for step in range(1, STEPS):
        for i in range(PIECES):
            piece = step * PIECES + i + AHEAD
            if piece < NPIECES:
                order.append(("x", piece))
            order += extras_after(step, i)
    return order


def extras_after(step, i):
    late = (step - (BATCH - 1)) * PIECES + i - 1
    if 0 <= late < PIECES:
        return [("w", 1, c, j) for c in range(CPP * late, CPP * late + CPP) for j in range(BANKS)]
    if step == BATCH + 1 and i == 0:
        return [("b", 1, j) for j in range(BANKS)]
    return []


def build(nc, x_pieces, x_rows, w_tiles, rt_tiles, lora_b, b_base, b_router, weight, bias_k, b2, cond_pack, out, spill):
    order = arrival_order()
    index = {item: n for n, item in enumerate(order)}
    behind = [index["x", 2 * PIECES] - 2 * PIECES,
              index["x", (BATCH + 2) * PIECES + AHEAD] - (BATCH + 2) * PIECES - AHEAD]

    def at(step, i):
        if isinstance(step, int):
            return index["x", step * PIECES + i]
        return None

    with ExitStack() as ctx:
        def sb(name, shape, dt=F32):
            return ctx.enter_context(nc.sbuf_tensor(name, shape, dt))

        def sem(name):
            return ctx.enter_context(nc.semaphore(name))

        w_hi = sb("w_hi", [P, CHUNKS, BANKS * BANK], F32R)
        w_lo = sb("w_lo", [P, CHUNKS, BANKS * BANK], F32R)
        rt_hl = sb("rt_hl", [P, CHUNKS, 2 * RT], F32R)
        b_hi = sb("b_hi", [ER, BANKS * BANK], F32R)
        b_lo = sb("b_lo", [ER, BANKS * BANK], F32R)
        raw = sb("raw", [P, RAW, RT_CH * RT])
        x_hi = sb("x_hi", [P, XSLOTS, PW], F32R)
        x_lo = sb("x_lo", [P, XSLOTS, PW], F32R)
        u_hi = sb("u_hi", [P, BANK], F32R)
        u_lo = sb("u_lo", [P, BANK], F32R)
        res = sb("res", [P, 2, BANKS, BANK])
        wsum_bc = sb("wsum_bc", [P, BANKS * BANK])
        bias_bc = sb("bias_bc", [P, BANKS * BANK])
        kern = sb("kern", [P, KERN, CH])
        mix = sb("mix", [P, CH])
        mix_hi = sb("mix_hi", [P, 2, CH], F32R)
        mix_lo = sb("mix_lo", [P, 2, CH], F32R)
        v_sb = sb("v_sb", [P, RT])
        v_hl = sb("v_hl", [P, 2, RT], F32R)
        low = sb("low", [P, RT])
        hw = sb("hw", [P, ER])
        hwt_hl = sb("hwt_hl", [P, 2, 2, P], F32R)
        ident = sb("ident", [P, P])
        ones_r = sb("ones_r", [P, P], F32R)
        rt_sum = sb("rt_sum", [P, RT])
        mixb = sb("mixb", [P, BATCH])
        att_bc = sb("att_bc", [P, BATCH * KERN])
        brt_bc = sb("brt_bc", [P, EXP])
        ranked = sb("ranked", [P, 3, 2 * EXP])
        inv_k = sb("inv_k", [P, EXP])
        tau = sb("tau", [P, 1])
        taus = sb("taus", [P, EXP])
        wts = sb("wts", [P, EXP])
        CP_W0, CP_W1, CP_W2 = BATCH, BATCH + P, BATCH + 2 * P
        CP_B0 = CP_W2 + KERN
        pack = sb("pack", [P, CP_B0 + 2])
        hid = sb("hid", [P, 2, BATCH])
        lg = sb("lg", [BATCH, KERN])
        lgs = sb("lgs", [BATCH, 2])
        b2_bc = sb("b2_bc", [BATCH, KERN])
        att_t = sb("att_t", [KERN, BATCH])
        att_d = sb("att_d", [KERN, BATCH, KERN])
        bk = sb("bk", [KERN, CH])

        ps_u = ctx.enter_context(nc.psum_tensor("ps_u", [P, 2, BANKS, BANK], F32))
        ps_o = ctx.enter_context(nc.psum_tensor("ps_o", [P, BANKS, BANK], F32))
        ps_v = ctx.enter_context(nc.psum_tensor("ps_v", [P, 2, BANK], F32))
        VAGG = 2 * RT

        raw_in = [sem(f"raw_in{s}") for s in range(RAW)]
        hi_done = sem("hi_done")
        split_done = sem("split_done")
        pieces_used = sem("pieces_used")
        wsum_done = sem("wsum_done")
        wsum_ready = sem("wsum_ready")
        rtsum_step = sem("rtsum_step")
        v_step = sem("v_step")
        v_ready = sem("v_ready")
        vmix_done = sem("vmix_done")
        uhi_done = sem("uhi_done")
        u_split = sem("u_split")
        route_step = sem("route_step")
        hw_ready = sem("hw_ready")
        hwt_done = sem("hwt_done")
        hwt_hi_done = sem("hwt_hi_done")
        hwt_split = sem("hwt_split")
        hwt_loaded = [sem(f"hwt_loaded{q}") for q in range(2)]
        spilled = [sem(f"spilled{q}") for q in range(2)]
        mix_step = sem("mix_step")
        mix_split = sem("mix_split")
        out_done = sem("out_done")
        fin_step = sem("fin_step")
        final_done = sem("final_done")
        res_in = [sem(f"res_in{q}") for q in range(2)]
        res_biased = sem("res_biased")
        stored = [[sem(f"stored{q}{j}") for j in range(BANKS)] for q in range(2)]
        bias_in = sem("bias_in")
        pack_in = sem("pack_in")
        small_in = sem("small_in")
        kern_in = sem("kern_in")
        const_step = sem("const_step")
        consts = sem("consts")
        c_mm = sem("c_mm")
        c_act = sem("c_act")
        c_dve = sem("c_dve")
        c_step = sem("c_step")

        block = ctx.enter_context(nc.Block())

        MIX_STEPS = KERN + 1
        ROUTE_STEPS = 10
        FORI = (1, BATCH // 2)
        SHORT = (1, BATCH // 2 - 1)

        def arrival(step, i, half):
            if isinstance(step, int):
                return index["x", step * PIECES + i + AHEAD]
            return step * PIECES + (i + AHEAD + behind[half])

        def arrival_slot(i, half):
            return (i + AHEAD + behind[half]) % RAW

        def raw_view(item):
            kind = item[0]
            s = index[item] % RAW
            if kind == "w":
                _, _, c, j = item
                cols = slice(j * BANK, (j + 1) * BANK)
                return raw[:, s, 0:BANK], w_hi[:, c, cols], w_lo[:, c, cols]
            if kind == "rt":
                cs = slice(item[1] * RT_CH, (item[1] + 1) * RT_CH)
                return (raw[:, s, :].rearrange("p (c n) -> p c n", n=RT), rt_hl[:, cs, 0:RT], rt_hl[:, cs, RT:2 * RT])
            if kind == "b":
                cols = slice(item[2] * BANK, (item[2] + 1) * BANK)
                return raw[:, s, 0:BANK], b_hi[:, cols], b_lo[:, cols]
            q = item[1] % XSLOTS
            return raw[:, s, 0:PW], x_hi[:, q, :], x_lo[:, q, :]

        @block.sync
        def _(sp):
            def load(n, slot, dst, src):
                if not isinstance(n, int) or n >= RAW:
                    sp.wait_ge(split_done, n - RAW + 1)
                sp.dma_start(dst, src).then_inc(raw_in[slot], 16)

            def load_item(item):
                n = index[item]
                kind = item[0]
                dst = raw_view(item)[0]
                if kind == "w":
                    src = w_tiles[item[1], item[2], item[3], :, :]
                elif kind == "rt":
                    src = rt_tiles[item[1], :, :].rearrange("p (c n) -> p c n", n=RT)
                elif kind == "b":
                    c0 = (item[1] * BANKS + item[2]) * BANK
                    src = lora_b[:, c0:c0 + BANK]
                else:
                    src = x_pieces[(item[1] // PIECES) % BATCH, item[1] % PIECES, :, :]
                load(n, n % RAW, dst, src)

            def load_step(m, par, half):
                step = m * 2 + par
                b = step - half * BATCH
                static = isinstance(m, int)
                for i in range(PIECES):
                    if static:
                        piece = step * PIECES + i + AHEAD
                        if piece < NPIECES:
                            load_item(("x", piece))
                        for item in extras_after(step, i):
                            load_item(item)
                    else:
                        over = (i + AHEAD) // PIECES
                        slot = arrival_slot(i, half)
                        src = x_pieces[bass.ds(b + over, 1), (i + AHEAD) % PIECES, :, :]
                        load(arrival(step, i, half), slot, raw[:, slot, 0:PW], src.rearrange("a p n -> p (a n)"))
                    if i == 4 and (not static or step - 1 >= BATCH) and half == 1:
                        q = (par + 1) % 2
                        pm = m - 1 + par
                        sp.wait_ge(out_done, step * 2 - 2 * BANKS + 0)
                        sp.wait_ge(spilled[q], BATCH // 2 * 16)
                        pb = step - 1 - BATCH
                        sp.dma_start(hwt_hl[:, q, :, :].rearrange("p a n -> p (a n)").bitcast(F32),
                                     spill[bass.ds(pb, 1), :, :].rearrange("a p n -> p (a n)")).then_inc(hwt_loaded[q], 16)

            sp.dma_start(pack[:, :], cond_pack).then_inc(pack_in, 16)
            sp.dma_start(b2_bc[:, :], b2.partition_broadcast(BATCH)).then_inc(small_in, 16)
            sp.dma_start(bk[:, :], bias_k).then_inc(small_in, 16)
            sp.dma_start(brt_bc[:, :], b_router.partition_broadcast(P)).then_inc(small_in, 16)
            first = order[:index["x", PIECES + AHEAD]]
            for n, item in enumerate(first):
                load_item(item)
                if n == 20:
                    sp.dma_start(kern[:, :, :], weight).then_inc(kern_in, 16)
            load_step(0, 1, 0)
            with sp.Fori(*SHORT) as k:
                load_step(k, 0, 0)
                load_step(k, 1, 0)
            load_step(BATCH // 2 - 1, 0, 0)
            load_step(BATCH // 2 - 1, 1, 0)
            load_step(BATCH // 2, 0, 1)
            load_step(BATCH // 2, 1, 1)
            with sp.Fori(*SHORT) as k:
                load_step(k + BATCH // 2, 0, 1)
                load_step(k + BATCH // 2, 1, 1)
            load_step(BATCH - 1, 0, 1)
            load_step(BATCH - 1, 1, 1)
            load_step(BATCH, 0, 1)
            for q in range(2):
                for j in range(BANKS):
                    sp.wait_ge(stored[q][j], STEPS // 2 * 16)

        @block.gpsimd
        def _(pool):
            nc.gpsimd.memset(ident[:, :], 0.0).then_inc(const_step, 1)
            pool.wait_ge(const_step, 1)
            nc.gpsimd.affine_select(out=ident[:, :], in_=ident[:, :], compare_op=ALU.not_equal, fill=1.0,
                                    base=0, pattern=[[-1, P]], channel_multiplier=1).then_inc(consts, 1)
            nc.gpsimd.memset(ones_r[:, :].bitcast(F32), 1.0).then_inc(consts, 1)
            nc.gpsimd.memset(ranked[:, :, :], 0.0).then_inc(consts, 1)
            for e in range(EXP):
                nc.gpsimd.memset(inv_k[:, e:e + 1], 1.0 / (e + 1)).then_inc(consts, 1)

            def add_bias(pm, q):
                pool.wait_ge(res_in[q], pm * 16 + 16)
                for j in range(BANKS):
                    nc.gpsimd.tensor_tensor(out=res[:, q, j, :], in0=res[:, q, j, :],
                                            in1=bias_bc[:, j * BANK:(j + 1) * BANK], op=ALU.add).then_inc(res_biased, 1)

            for half in range(HALVES):
                if half:
                    pool.wait_ge(res_biased, BATCH * BANKS)
                c0 = half * BANKS * BANK
                pool.dma_start(bias_bc[:, :], b_base[c0:c0 + BANKS * BANK].partition_broadcast(P)).then_inc(bias_in, 16)
                pool.wait_ge(bias_in, 16 * half + 16)
                with pool.Fori(0, BATCH // 2) as k:
                    add_bias(k + half * (BATCH // 2), 0)
                    add_bias(k + half * (BATCH // 2), 1)

        @block.scalar
        def _(act):
            def hi_item(item):
                n = index[item]
                src, hi, _ = raw_view(item)
                act.wait_ge(raw_in[n % RAW], (n // RAW + 1) * 16)
                if item[0] == "x" and item[1] >= XSLOTS:
                    act.wait_ge(pieces_used, item[1] - XSLOTS + 1)
                if item[0] == "w" and item[1] == 1:
                    act.wait_ge(pieces_used, (BATCH - 1) * PIECES + item[2] // CPP + 1)
                if item[0] == "b" and item[1] == 1:
                    act.wait_ge(out_done, BATCH * BANKS)
                nc.scalar.activation(hi, src, ACT.Copy).then_inc(hi_done, 1)

            def load_rows(m, par, b, half):
                for j in range(BANKS):
                    if not isinstance(m, int) or m >= 1:
                        act.wait_ge(stored[par][j], m * 16)
                c0 = half * BANKS * BANK
                act.dma_start(res[:, par, :, :].rearrange("p a n -> p (a n)"),
                              x_rows[bass.ds(b, 1), :, c0:c0 + BANKS * BANK].rearrange("a p n -> p (a n)"))\
                   .then_inc(res_in[par], 16)

            def hi_step(m, par, half):
                static = isinstance(m, int)
                step = m * 2 + par
                q = (par + 1) % 2
                pm = m - 1 + par
                prev = step - 1
                phalf = prev // BATCH if static else half
                pb = prev % BATCH if static else prev - half * BATCH
                last = static and step == STEPS

                def store(j, q, pb, phalf, count):
                    act.wait_ge(final_done, count)
                    c0 = (phalf * BANKS + j) * BANK
                    act.dma_start(out[bass.ds(pb, 1), :, c0:c0 + BANK].rearrange("a p n -> p (a n)"), res[:, q, j, :])\
                       .then_inc(stored[q][j], 16)

                for i in range(PIECES):
                    if static:
                        piece = step * PIECES + i + AHEAD
                        if piece < NPIECES:
                            hi_item(("x", piece))
                        for item in extras_after(step, i):
                            hi_item(item)
                    else:
                        slot = arrival_slot(i, half)
                        xs = (i + AHEAD) % XSLOTS
                        lap = (i + AHEAD + behind[half]) // RAW + 1
                        act.wait_ge(raw_in[slot], (step * (PIECES // RAW) + lap) * 16)
                        act.wait_ge(pieces_used, step * PIECES + (i + AHEAD - XSLOTS + 1))
                        nc.scalar.activation(x_hi[:, xs, :], raw[:, slot, 0:PW], ACT.Copy).then_inc(hi_done, 1)
                    if i == 0:
                        if static and step == 1:
                            act.wait_ge(wsum_done, 1)
                            nc.scalar.activation(wsum_bc[:, :], ps_o[:, :, :].rearrange("p a n -> p (a n)"), ACT.Copy)\
                              .then_inc(wsum_ready, 1)
                        act.wait_ge(pieces_used, step * PIECES)
                        if not static or prev >= 1:
                            act.wait_ge(out_done, prev * BANKS)
                        nc.scalar.activation(u_hi[:, :], ps_u[:, q, 0, :], ACT.Copy).then_inc(uhi_done, 1)
                    if i == 1 and (not static or prev >= 1):
                        p2 = prev - 1
                        store(1, par, p2 % BATCH if static else p2 - half * BATCH, p2 // BATCH if static else half, prev * BANKS)
                    if i == 3 and phalf == 0:
                        act.wait_ge(hwt_done, prev + 1)
                        if not static or pm >= 1:
                            act.wait_ge(spilled[q], pm * 16)
                        nc.scalar.activation(hwt_hl[:, q, 0, :], ps_v[:, q, 0:P], ACT.Copy).then_inc(hwt_hi_done, 1)
                    if i == 4 and not last:
                        load_rows(m, par, step % BATCH if static else step - half * BATCH, half)
                    if i == 4 and static and step == BATCH + 1:
                        act.wait_ge(wsum_done, 2)
                        act.wait_ge(final_done, BATCH * BANKS)
                        nc.scalar.activation(wsum_bc[:, :], ps_v[:, :, :].rearrange("p a n -> p (a n)"), ACT.Copy)\
                          .then_inc(wsum_ready, 1)
                    if i == 5:
                        act.wait_ge(out_done, prev * BANKS + 1)
                        nc.scalar.activation(u_hi[:, :], ps_u[:, q, 1, :], ACT.Copy).then_inc(uhi_done, 1)
                        if phalf == 0:
                            act.wait_ge(hwt_split, prev + 1)
                            act.dma_start(spill[bass.ds(pb, 1), :, :].rearrange("a p n -> p (a n)"),
                                          hwt_hl[:, q, :, :].rearrange("p a n -> p (a n)").bitcast(F32)).then_inc(spilled[q], 16)
                    if i == 7:
                        store(0, q, pb, phalf, prev * BANKS + 1)
                        if last:
                            store(1, q, pb, phalf, prev * BANKS + 2)

            first = order[:index["x", PIECES + AHEAD]]
            for item in first:
                hi_item(item)
                if item == ("w", 0, 2 * CPP + 1, 1):
                    act.wait_ge(c_mm, 1)
                    nc.scalar.activation(hid[:, 0, :], ps_u[:, 1, 0, 0:BATCH], ACT.Gelu,
                                         bias=pack[:, CP_B0:CP_B0 + 1]).then_inc(c_act, 1)
                if item == ("w", 0, 3 * CPP + 1, 1):
                    act.wait_ge(c_mm, 2)
                    nc.scalar.activation(hid[:, 1, :], ps_u[:, 1, 0, 0:BATCH], ACT.Gelu,
                                         bias=pack[:, CP_B0 + 1:CP_B0 + 2]).then_inc(c_act, 1)
                if item == ("w", 0, 4 * CPP + 1, 1):
                    act.wait_ge(c_dve, 1)
                    nc.scalar.activation(lg[:, :], lg[:, :], ACT.Exp).then_inc(c_act, 1)
            load_rows(0, 0, 0, 0)
            hi_step(0, 1, 0)
            with act.Fori(*SHORT) as k:
                hi_step(k, 0, 0)
                hi_step(k, 1, 0)
            hi_step(BATCH // 2 - 1, 0, 0)
            hi_step(BATCH // 2 - 1, 1, 0)
            hi_step(BATCH // 2, 0, 1)
            hi_step(BATCH // 2, 1, 1)
            with act.Fori(*SHORT) as k:
                hi_step(k + BATCH // 2, 0, 1)
                hi_step(k + BATCH // 2, 1, 1)
            hi_step(BATCH - 1, 0, 1)
            hi_step(BATCH - 1, 1, 1)
            hi_step(BATCH, 0, 1)

        @block.vector
        def _(dve):
            def minus(out, a, hi):
                return nc.vector.tensor_tensor(out=out, in0=a, in1=hi.bitcast(F32), op=ALU.subtract)

            def lo_item(item):
                n = index[item]
                src, hi, lo = raw_view(item)
                dve.wait_ge(hi_done, n + 1)
                minus(lo, src, hi).then_inc(split_done, 1)

            def mix_kernels(step, b, par, static):
                base = step * MIX_STEPS
                if not static or step >= 2:
                    dve.wait_ge(out_done, (step - 1) * BANKS)
                for k in range(KERN):
                    coef = att_bc[:, bass.ds(b * KERN + k, 1)]
                    if k == 0:
                        nc.vector.tensor_scalar(mix[:, :], kern[:, k, :], coef, None, ALU.mult).then_inc(mix_step, 1)
                    else:
                        nc.vector.scalar_tensor_tensor(out=mix[:, :], in0=kern[:, k, :], scalar=coef, in1=mix[:, :],
                                                       op0=ALU.mult, op1=ALU.add).then_inc(mix_step, 1)
                    dve.wait_ge(mix_step, base + (k + 1))
                nc.vector.tensor_copy(mix_hi[:, par, :], mix[:, :]).then_inc(mix_step, 1)
                dve.wait_ge(mix_step, base + MIX_STEPS)
                minus(mix_lo[:, par, :], mix[:, :], mix_hi[:, par, :]).then_inc(mix_split, 1)

            def split_v(prev, q):
                base = prev * 3
                nc.vector.tensor_copy(v_sb[:, :], ps_v[:, q, RT:2 * RT]).then_inc(v_step, 1)
                dve.wait_ge(v_step, base + 1)
                nc.vector.tensor_tensor(out=v_sb[:, :], in0=ps_v[:, q, 0:RT], in1=v_sb[:, :], op=ALU.add).then_inc(v_step, 1)
                dve.wait_ge(v_step, base + 2)
                nc.vector.tensor_copy(v_hl[:, 0, :], v_sb[:, :]).then_inc(v_step, 1)
                dve.wait_ge(v_step, base + 3)
                minus(v_hl[:, 1, :], v_sb[:, :], v_hl[:, 0, :]).then_inc(v_ready, 1)

            def route(prev, pb, q):
                base = prev * ROUTE_STEPS
                stage = [0]

                def then(ins):
                    stage[0] += 1
                    ins.then_inc(route_step, 1)
                    dve.wait_ge(route_step, base + stage[0])

                dve.wait_ge(vmix_done, prev + 1)
                def mixed(cols):
                    return nc.vector.scalar_tensor_tensor(
                        out=low[:, cols], in0=rt_sum[:, cols], scalar=mixb[:, bass.ds(pb, 1)],
                        in1=ps_v[:, q, VAGG + cols.start:VAGG + cols.stop], op0=ALU.mult, op1=ALU.add)

                logits = low[:, ER:RT]
                then(mixed(slice(ER, RT)))
                then(nc.vector.tensor_tensor(out=logits, in0=logits, in1=brt_bc[:, :], op=ALU.add))
                stage[0] += 1
                mixed(slice(0, ER)).then_inc(route_step, 1)
                dve.wait_ge(consts, 3 + EXP)
                then(nc.vector.max(ranked[:, 0, EXP:2 * EXP], logits))
                for s, (a, o) in zip((1, 2, 4), ((0, 1), (1, 2), (2, 0))):
                    dst = taus[:, :] if s == 4 else ranked[:, o, EXP:2 * EXP]
                    then(nc.vector.tensor_tensor(out=dst, in0=ranked[:, a, EXP:2 * EXP],
                                                 in1=ranked[:, a, EXP - s:2 * EXP - s], op=ALU.add))
                then(nc.vector.scalar_tensor_tensor(out=taus[:, :], in0=taus[:, :], scalar=-1.0, in1=inv_k[:, :],
                                                    op0=ALU.add, op1=ALU.mult))
                then(nc.vector.reduce_max(tau[:, :], taus[:, :], AX.X))
                then(nc.vector.tensor_scalar(wts[:, :], logits, tau[:, 0:1], 0.0, ALU.subtract, ALU.max))
                nc.vector.tensor_tensor(out=hw[:, :].rearrange("p (e r) -> p e r", r=RANK),
                                        in0=low[:, 0:ER].rearrange("p (e r) -> p e r", r=RANK),
                                        in1=wts[:, :].unsqueeze(2).broadcast_to([P, EXP, RANK]), op=ALU.mult)\
                  .then_inc(hw_ready, 1)

            def split_u(j, q, prev):
                dve.wait_ge(uhi_done, prev * BANKS + j + 1)
                minus(u_lo[:, :], ps_u[:, q, j, :], u_hi[:, :]).then_inc(u_split, 1)

            def finish(j, q, prev, pb):
                dve.wait_ge(out_done, prev * BANKS + j + 1)
                nc.vector.scalar_tensor_tensor(out=ps_o[:, j, :], in0=wsum_bc[:, j * BANK:(j + 1) * BANK],
                                               scalar=mixb[:, bass.ds(pb, 1)], in1=ps_o[:, j, :],
                                               op0=ALU.mult, op1=ALU.add).then_inc(fin_step, 1)
                dve.wait_ge(fin_step, prev * BANKS + j + 1)
                dve.wait_ge(res_biased, prev * BANKS + j + 1)
                nc.vector.tensor_tensor(out=res[:, q, j, :], in0=res[:, q, j, :], in1=ps_o[:, j, :], op=ALU.add)\
                  .then_inc(final_done, 1)

            def lo_step(m, par, half):
                static = isinstance(m, int)
                step = m * 2 + par
                q = (par + 1) % 2
                prev = step - 1
                phalf = prev // BATCH if static else half
                pb = prev % BATCH if static else prev - half * BATCH
                for i in range(PIECES):
                    if static:
                        piece = step * PIECES + i + AHEAD
                        if piece < NPIECES:
                            lo_item(("x", piece))
                        for item in extras_after(step, i):
                            lo_item(item)
                    else:
                        slot = arrival_slot(i, half)
                        xs = (i + AHEAD) % XSLOTS
                        dve.wait_ge(hi_done, step * PIECES + (i + AHEAD + behind[half] + 1))
                        minus(x_lo[:, xs, :], raw[:, slot, 0:PW], x_hi[:, xs, :]).then_inc(split_done, 1)
                    if i == 0:
                        if phalf == 0:
                            dve.wait_ge(pieces_used, step * PIECES)
                            split_v(prev, q)
                        split_u(0, q, prev)
                    if i == 1 and phalf == 0:
                        route(prev, pb, q)
                    if i == 2 and not (static and step == STEPS):
                        mix_kernels(step, step % BATCH if static else step - half * BATCH, par, static)
                    if i == 3 and phalf == 0:
                        dve.wait_ge(hwt_hi_done, prev + 1)
                        minus(hwt_hl[:, q, 1, :], ps_v[:, q, 0:P], hwt_hl[:, q, 0, :]).then_inc(hwt_split, 1)
                    if i == 5:
                        split_u(1, q, prev)
                        if static and step == 1:
                            dve.wait_ge(wsum_ready, 1)
                        if static and step == BATCH + 1:
                            dve.wait_ge(wsum_ready, 2)
                        finish(0, q, prev, pb)
                    if i == 7:
                        finish(1, q, prev, pb)

            first = order[:index["x", PIECES + AHEAD]]
            for item in first:
                lo_item(item)
                if item == ("w", 0, 4 * CPP + 1, 1):
                    dve.wait_ge(c_mm, 3)
                    dve.wait_ge(small_in, 48)
                    nc.vector.tensor_tensor(out=lg[:, :], in0=ps_u[0:BATCH, 1, 0, 0:KERN], in1=b2_bc[:, :], op=ALU.add)\
                      .then_inc(c_step, 1)
                    dve.wait_ge(c_step, 1)
                    nc.vector.reduce_max(lgs[:, 0:1], lg[:, :], AX.X).then_inc(c_step, 1)
                    dve.wait_ge(c_step, 2)
                    nc.vector.tensor_scalar(lg[:, :], lg[:, :], lgs[:, 0:1], None, ALU.subtract).then_inc(c_dve, 1)
                if item == ("w", 0, 5 * CPP + 1, 1):
                    dve.wait_ge(c_act, 3)
                    nc.vector.reduce_sum(lgs[:, 0:1], lg[:, :], AX.X).then_inc(c_step, 1)
                    dve.wait_ge(c_step, 3)
                    nc.vector.reciprocal(lgs[:, 1:2], lgs[:, 0:1]).then_inc(c_step, 1)
                    dve.wait_ge(c_step, 4)
                    nc.vector.tensor_scalar(lg[:, :], lg[:, :], lgs[:, 1:2], None, ALU.mult).then_inc(c_dve, 1)
            dve.wait_ge(c_mm, 4)
            nc.vector.tensor_copy(att_t[:, :], ps_u[0:KERN, 1, 0, 0:BATCH]).then_inc(c_step, 1)
            dve.wait_ge(c_step, 5)
            nc.vector.tensor_tensor(out=att_d[:, :, :], in0=att_t[:, :].unsqueeze(2).broadcast_to([KERN, BATCH, KERN]),
                                    in1=ident[0:KERN, 0:KERN].unsqueeze(1).broadcast_to([KERN, BATCH, KERN]),
                                    op=ALU.mult).then_inc(c_dve, 1)
            dve.wait_ge(c_mm, 5)
            nc.vector.tensor_copy(att_bc[:, :], ps_u[:, 1, 0, 0:BATCH * KERN]).then_inc(c_step, 1)
            nc.vector.tensor_copy(mixb[:, :], ps_u[:, 1, 1, 0:BATCH]).then_inc(c_dve, 1)
            dve.wait_ge(c_step, 6)
            dve.wait_ge(c_dve, 4)
            dve.wait_ge(kern_in, 16)
            mix_kernels(0, 0, 0, True)
            dve.wait_ge(wsum_done, 1)
            nc.vector.tensor_copy(rt_sum[:, :], ps_v[:, 1, RT:2 * RT]).then_inc(rtsum_step, 1)
            dve.wait_ge(rtsum_step, 1)
            nc.vector.tensor_tensor(out=rt_sum[:, :], in0=ps_v[:, 1, 0:RT], in1=rt_sum[:, :], op=ALU.add)\
              .then_inc(rtsum_step, 1)
            dve.wait_ge(rtsum_step, 2)
            lo_step(0, 1, 0)
            with dve.Fori(*SHORT) as k:
                lo_step(k, 0, 0)
                lo_step(k, 1, 0)
            lo_step(BATCH // 2 - 1, 0, 0)
            lo_step(BATCH // 2 - 1, 1, 0)
            lo_step(BATCH // 2, 0, 1)
            lo_step(BATCH // 2, 1, 1)
            with dve.Fori(*SHORT) as k:
                lo_step(k + BATCH // 2, 0, 1)
                lo_step(k + BATCH // 2, 1, 1)
            lo_step(BATCH - 1, 0, 1)
            lo_step(BATCH - 1, 1, 1)
            lo_step(BATCH, 0, 1)

        @block.tensor
        def _(pe):
            mm = nc.tensor.matmul

            def chunk(c, par, half):
                xs, xc = (c // CPP) % XSLOTS, slice(c % CPP * CH, (c % CPP + 1) * CH)
                hi, lo = x_hi[:, xs, xc], x_lo[:, xs, xc]
                first, last = c == 0, c == CHUNKS - 1
                for j in range(BANKS):
                    mm(ps_u[:, par, j, :], hi, w_hi[:, c, j * BANK:(j + 1) * BANK], start=first, stop=False)
                for j in range(BANKS):
                    mm(ps_u[:, par, j, :], hi, w_lo[:, c, j * BANK:(j + 1) * BANK], start=False, stop=False)
                if half == 0:
                    mm(ps_v[:, par, 0:2 * RT], hi, rt_hl[:, c, :], start=first, stop=False, skip_group_check=True)
                    mm(ps_v[:, par, RT:2 * RT], lo, rt_hl[:, c, 0:RT], start=False, stop=last, skip_group_check=True)
                for j in range(BANKS):
                    ins = mm(ps_u[:, par, j, :], lo, w_hi[:, c, j * BANK:(j + 1) * BANK], start=False, stop=last)
                return ins

            def split_product(dst, a_hi, a_lo, b_hi_, b_lo_, start, stop):
                mm(dst, a_hi, b_hi_, start=start, stop=False)
                mm(dst, a_hi, b_lo_, start=False, stop=False)
                return mm(dst, a_lo, b_hi_, start=False, stop=stop)

            def col_sums(dst, c, first, last):
                for j in range(BANKS):
                    mm(dst[:, j, :], ones_r[:, :], w_hi[:, c, j * BANK:(j + 1) * BANK], start=first, stop=False)
                    ins = mm(dst[:, j, :], ones_r[:, :], w_lo[:, c, j * BANK:(j + 1) * BANK], start=False, stop=last)
                return ins

            def out_bank(j, m, par, static, step, phalf):
                q = (par + 1) % 2
                pm = m - 1 + par
                prev = step - 1
                cols = slice(j * BANK, (j + 1) * BANK)
                pe.wait_ge(u_split, prev * BANKS + j + 1)
                if not static or prev >= 1:
                    pe.wait_ge(final_done, (prev - 1) * BANKS + j + 1)
                if static and prev == 0 and j == 0:
                    pe.wait_ge(wsum_ready, 1)
                if j == 0:
                    pe.wait_ge(mix_split, prev + 1)
                    if phalf == 0:
                        pe.wait_ge(hwt_split, prev + 1)
                    else:
                        pe.wait_ge(hwt_loaded[q], (pm - BATCH // 2 + 1) * 16)
                if static and prev % BATCH == 0:
                    pe.wait_ge(split_done, index["b", prev // BATCH, j] + 1)
                split_product(ps_o[:, j, :], mix_hi[:, q, :], mix_lo[:, q, :], u_hi[:, :], u_lo[:, :], True, False)
                split_product(ps_o[:, j, :], hwt_hl[:, q, 0, :], hwt_hl[:, q, 1, :], b_hi[:, cols], b_lo[:, cols],
                              False, True).then_inc(out_done, 1)

            def mm_step(m, par, half):
                static = isinstance(m, int)
                step = m * 2 + par
                q = (par + 1) % 2
                prev = step - 1
                phalf = prev // BATCH if static else half
                has_prev = not static or step > 0
                has_base = not static or step < STEPS
                for i in range(PIECES):
                    if has_base:
                        if static:
                            pe.wait_ge(split_done, index["x", step * PIECES + i] + 1)
                        else:
                            pe.wait_ge(split_done, step * PIECES + (i + behind_at(half, i) + 1))
                        for c in range(i * CPP, i * CPP + CPP):
                            if static and step % BATCH == 0:
                                pe.wait_ge(split_done, index["w", half, c, BANKS - 1] + 1)
                            ins = chunk(c, par, half)
                            if static and step == 0:
                                ins2 = col_sums(ps_o, c, c == 0, c == CHUNKS - 1)
                                ins2 = mm(ps_v[:, 1, 0:2 * RT], ones_r[:, :], rt_hl[:, c, :], start=(c == 0), stop=(c == CHUNKS - 1))
                                if c == CHUNKS - 1:
                                    ins2.then_inc(wsum_done, 1)
                        ins.then_inc(pieces_used, 1)
                    if static and step == BATCH + 1 and i < CHUNKS // 4:
                        for c in range(4 * i, 4 * i + 4):
                            ins2 = col_sums(ps_v, c, c == 0, c == CHUNKS - 1)
                        if i == CHUNKS // 4 - 1:
                            ins2.then_inc(wsum_done, 1)
                    if static and step == 0:
                        attention(i)
                    if not has_prev:
                        continue
                    if i == 0 and phalf == 0:
                        pe.wait_ge(v_ready, prev + 1)
                        pe.wait_ge(mix_split, prev + 1)
                        split_product(ps_v[:, q, VAGG:VAGG + RT], mix_hi[:, q, :], mix_lo[:, q, :], v_hl[:, 0, :], v_hl[:, 1, :],
                                      True, True).then_inc(vmix_done, 1)
                    if i == 2 and phalf == 0:
                        pe.wait_ge(hw_ready, prev + 1)
                        nc.tensor.transpose(ps_v[:, q, 0:P], hw[:, :], ident[:, :]).then_inc(hwt_done, 1)
                    if i == 4:
                        out_bank(0, m, par, static, step, phalf)
                    if i == 6:
                        out_bank(1, m, par, static, step, phalf)

            def behind_at(half, i):
                return behind[half]

            def attention(i):
                small = ps_u[:, 1, 0, :]
                if i == 0:
                    pe.wait_ge(pack_in, 16)
                    mm(small[:, 0:BATCH], pack[:, CP_W0:CP_W1], pack[:, 0:BATCH], start=True, stop=True).then_inc(c_mm, 1)
                if i == 3:
                    pe.wait_ge(c_act, 1)
                    mm(small[:, 0:BATCH], pack[:, CP_W1:CP_W2], hid[:, 0, :], start=True, stop=True).then_inc(c_mm, 1)
                if i == 4:
                    pe.wait_ge(c_act, 2)
                    mm(small[0:BATCH, 0:KERN], hid[:, 1, :], pack[:, CP_W2:CP_B0], start=True, stop=True).then_inc(c_mm, 1)
                if i == 6:
                    pe.wait_ge(c_dve, 2)
                    pe.wait_ge(consts, 3 + EXP)
                    nc.tensor.transpose(small[0:KERN, 0:BATCH], lg[:, :], ident[0:BATCH, 0:BATCH]).then_inc(c_mm, 1)
                if i == 7:
                    pe.wait_ge(c_dve, 3)
                    pe.wait_ge(small_in, 48)
                    mm(ps_u[:, 1, 1, 0:BATCH], bk[:, :], att_t[:, :], start=True, stop=True)
                    mm(small[:, 0:BATCH * KERN], ones_r[0:KERN, :].bitcast(F32), att_d[:, :, :].rearrange("k b n -> k (b n)"),
                       start=True, stop=True).then_inc(c_mm, 1)

            pe.wait_ge(consts, 3 + EXP)
            mm_step(0, 0, 0)
            pe.wait_ge(c_dve, 4)
            pe.wait_ge(c_step, 6)
            pe.wait_ge(rtsum_step, 2)
            mm_step(0, 1, 0)
            with pe.Fori(*FORI) as k:
                mm_step(k, 0, 0)
                mm_step(k, 1, 0)
            mm_step(BATCH // 2, 0, 1)
            mm_step(BATCH // 2, 1, 1)
            with pe.Fori(*FORI) as k:
                mm_step(k + BATCH // 2, 0, 1)
                mm_step(k + BATCH // 2, 1, 1)
            mm_step(BATCH, 0, 1)


def kernel(**inputs):
    import numpy as np
    import concourse.bacc as bacc
    from concourse.bass_utils import run_bass_kernel_spmd

    a = {k: np.asarray(v) for k, v in inputs.items()}
    x = a["x"]
    low = np.concatenate([a["L0_ffn_lora_A"].transpose(1, 0, 2).reshape(HID, ER), a["L0_ffn_W_router"].T], axis=1)
    laid = {
        "x_pieces": x.reshape(BATCH, CH, PIECES, CPP, P).transpose(0, 2, 4, 3, 1).reshape(BATCH, PIECES, P, PW),
        "x_rows": x,
        "w_tiles": a["L0_ffn_W_base"].reshape(HALVES, BANKS, BANK, CHUNKS, P).transpose(0, 3, 1, 4, 2),
        "rt_tiles": low.reshape(CHUNKS // RT_CH, RT_CH, P, RT).transpose(0, 2, 1, 3).reshape(CHUNKS // RT_CH, P, RT_CH * RT),
        "lora_b": a["L0_ffn_lora_B"].reshape(ER, DOUT),
        "b_base": a["L0_ffn_b_base"],
        "b_router": a["L0_ffn_b_router"],
        "weight": a["L0_cond_weight"][..., 0].transpose(2, 0, 1),
        "bias_k": a["L0_cond_bias_k"],
        "b2": a["L0_cond_b2"],
        "cond_pack": np.concatenate([a["cond_128"].T, a["L0_cond_W0"], a["L0_cond_W1"], a["L0_cond_W2"],
                                     a["L0_cond_b0"][:, None], a["L0_cond_b1"][:, None]], axis=1),
    }
    nc = bacc.Bacc("TRN2", target_bir_lowering=False, num_devices=1)
    arrays, args = {}, []
    for name, v in laid.items():
        v = np.ascontiguousarray(v)
        arrays[f"in_{name}"] = v
        args.append(nc.dram_tensor(f"in_{name}", v.shape, mybir.dt.from_np(v.dtype), kind="ExternalInput").ap())
    args.append(nc.dram_tensor("out_0", (BATCH, CH, DOUT), F32, kind="ExternalOutput").ap())
    args.append(nc.dram_tensor("hwt_spill", (BATCH, P, 2 * P), F32, kind="Internal").ap())
    build(nc, *args)
    r = run_bass_kernel_spmd(nc, [arrays], core_ids=[0])
    return r.results[0]["out_0"]
```

```python
import concourse.bass as bass
from concourse import mybir
from contextlib import ExitStack

F32 = mybir.dt.float32
F32R = mybir.dt.float32r
ALU = mybir.AluOpType
ACT = mybir.ActivationFunctionType
AX = mybir.AxisListType

BATCH = 32
CH = 128
HID = 2048
DOUT = 2048
EXP = 8
RANK = 16
KERN = 8
P = 128

ER = EXP * RANK
RT = ER + EXP
HALVES = 2
BANK = 512
BANKS = DOUT // HALVES // BANK
CHUNKS = HID // P
CPP = 2
PIECES = CHUNKS // CPP
PW = CPP * CH
XSLOTS = 4
RAW = 8
WR = BANKS * BANK + RT
TILES = 2
WIDE = [WR // TILES, BANKS * BANK // TILES]
ROW_TILES = 2 * BANKS * BANK // P
ROW_W = HID * BANKS * BANK // P // ROW_TILES
SEGS = [[(0, 388), (388, 776), (776, WR)], [(0, BANK), (BANK, 2 * BANK)]]
VCOL = BANKS * BANK
VBANK = len(SEGS[0]) - 1
SEG_TOTAL = [0, BATCH * len(SEGS[0])]
AHEAD = 3
STEPS = HALVES * BATCH
NPIECES = STEPS * PIECES


def arrival_order():
    order = []
    for i in range(PIECES):
        order.append(("x", i))
        order += [("w", 0, c, j) for c in range(CPP * i, CPP * i + CPP) for j in range(TILES)]
    order += [("x", PIECES + i) for i in range(AHEAD)]
    order += [("b", 0, j) for j in range(BANKS)]
    for step in range(1, STEPS):
        for i in range(PIECES):
            piece = step * PIECES + i + AHEAD
            if piece < NPIECES:
                order.append(("x", piece))
            order += extras_after(step, i)
    return order


def extras_after(step, i):
    slot = (step - (BATCH - 1)) * PIECES + i - 1
    if 0 <= slot < 2 * PIECES:
        chunks = range(min(slot * 5 // 4, CHUNKS), min((slot + 1) * 5 // 4, CHUNKS))
        return [("w", 1, c, j) for c in chunks for j in range(TILES)]
    if step == BATCH + 1 and i == 1:
        return [("b", 1, j) for j in range(BANKS)]
    return []


def build(nc, x_pieces, x_rows, w_tiles0, w_tiles1, w_rows, lora_b, b_base, b_router, weight, bias_k, b2, cond_pack, out, spill):
    order = arrival_order()
    index = {item: n for n, item in enumerate(order)}
    behind = [index["x", 2 * PIECES] - 2 * PIECES,
              index["x", (BATCH + 2) * PIECES + AHEAD] - (BATCH + 2) * PIECES - AHEAD]

    with ExitStack() as ctx:
        def sb(name, shape, dt=F32):
            return ctx.enter_context(nc.sbuf_tensor(name, shape, dt))

        def sem(name):
            return ctx.enter_context(nc.semaphore(name))

        w_hi = sb("w_hi", [P, CHUNKS, WR], F32R)
        w_lo = sb("w_lo", [P, CHUNKS, WR], F32R)
        b_hi = sb("b_hi", [ER, BANKS * BANK], F32R)
        b_lo = sb("b_lo", [ER, BANKS * BANK], F32R)
        raw = sb("raw", [P, RAW, WIDE[0]])
        x_hi = sb("x_hi", [P, XSLOTS, PW], F32R)
        x_lo = sb("x_lo", [P, XSLOTS, PW], F32R)
        uv_hi = sb("uv_hi", [P, WR], F32R)
        uv_lo = sb("uv_lo", [P, WR], F32R)
        res = sb("res", [P, 2, BANKS, BANK])
        wsum_bc = sb("wsum_bc", [P, BANKS * BANK])
        bias_bc = sb("bias_bc", [P, BANKS * BANK])
        rows = sb("rows", [P, ROW_W])
        row_sum = sb("row_sum", [P, ROW_TILES])
        tots = sb("tots", [P, ROW_TILES // 2])
        kern = sb("kern", [P, KERN, CH])
        mix = sb("mix", [P, CH])
        mix_hi = sb("mix_hi", [P, 2, CH], F32R)
        mix_lo = sb("mix_lo", [P, 2, CH], F32R)
        low = sb("low", [P, RT])
        hw = sb("hw", [P, ER])
        hwt_hl = sb("hwt_hl", [P, 2, P], F32R)
        ident = sb("ident", [P, P])
        ones_r = sb("ones_r", [P, P], F32R)
        rt_sum = sb("rt_sum", [P, RT])
        mixb = sb("mixb", [P, BATCH])
        att_bc = sb("att_bc", [P, BATCH * KERN])
        brt_bc = sb("brt_bc", [P, EXP])
        ranked = sb("ranked", [P, 3, 2 * EXP])
        inv_k = sb("inv_k", [P, EXP])
        tau = sb("tau", [P, 1])
        taus = sb("taus", [P, EXP])
        wts = sb("wts", [P, EXP])
        CP_W0, CP_W1, CP_W2 = BATCH, BATCH + P, BATCH + 2 * P
        CP_B0 = CP_W2 + KERN
        spare = [0]

        def early(rows, cols):
            spare[0] += cols
            return wsum_bc[0:rows, spare[0] - cols:spare[0]]

        pack = early(P, CP_B0 + 2)
        hid = early(P, 2 * BATCH).rearrange("p (a n) -> p a n", a=2)
        lg = early(BATCH, KERN)
        lgs = early(BATCH, 2)
        b2_bc = early(BATCH, KERN)
        att_t = early(KERN, BATCH)
        att_d = early(KERN, BATCH * KERN).rearrange("k (b n) -> k b n", n=KERN)
        bk = early(KERN, CH)

        ps_u = ctx.enter_context(nc.psum_tensor("ps_u", [P, 2, len(SEGS[0]), BANK], F32))
        ps_o = ctx.enter_context(nc.psum_tensor("ps_o", [P, BANKS, BANK], F32))
        HWT = 2 * P

        raw_in = [sem(f"raw_in{s}") for s in range(RAW)]
        hi_done = sem("hi_done")
        split_done = sem("split_done")
        pieces_used = sem("pieces_used")
        wsum_done = sem("wsum_done")
        wsum_ready = sem("wsum_ready")
        rtsum_ready = sem("rtsum_ready")
        rows_in = sem("rows_in")
        rows_summed = sem("rows_summed")
        rows_step = sem("rows_step")
        vmix_done = sem("vmix_done")
        uhi_done = sem("uhi_done")
        u_split = sem("u_split")
        route_step = sem("route_step")
        hw_ready = sem("hw_ready")
        hwt_done = sem("hwt_done")
        hwt_hi_done = sem("hwt_hi_done")
        hwt_split = sem("hwt_split")
        hwt_loaded = sem("hwt_loaded")
        spilled = sem("spilled")
        mix_step = sem("mix_step")
        mix_split = sem("mix_split")
        out_done = sem("out_done")
        fin_step = sem("fin_step")
        final_done = sem("final_done")
        res_in = [sem(f"res_in{q}") for q in range(2)]
        res_biased = sem("res_biased")
        stored = [[sem(f"stored{q}{j}") for j in range(BANKS)] for q in range(2)]
        bias_in = sem("bias_in")
        pack_in = sem("pack_in")
        small_in = sem("small_in")
        kern_in = sem("kern_in")
        const_step = sem("const_step")
        consts = sem("consts")
        c_mm = sem("c_mm")
        c_act = sem("c_act")
        c_dve = sem("c_dve")
        c_step = sem("c_step")

        block = ctx.enter_context(nc.Block())

        MIX_STEPS = KERN + 1
        ROUTE_STEPS = 10
        PAIRS = (1, BATCH // 2 - 1)

        def arrival(step, i, half):
            return step * PIECES + (i + AHEAD + behind[half])

        def arrival_slot(i, half):
            return (i + AHEAD + behind[half]) % RAW

        def raw_view(item):
            kind = item[0]
            s = index[item] % RAW
            if kind == "w":
                _, half, c, j = item
                cols = slice(j * WIDE[half], (j + 1) * WIDE[half])
                return raw[:, s, 0:WIDE[half]], w_hi[:, c, cols], w_lo[:, c, cols]
            if kind == "b":
                cols = slice(item[2] * BANK, (item[2] + 1) * BANK)
                return raw[:, s, 0:BANK], b_hi[:, cols], b_lo[:, cols]
            q = item[1] % XSLOTS
            return raw[:, s, 0:PW], x_hi[:, q, :], x_lo[:, q, :]

        def row_tile(m, par):
            if not isinstance(m, int):
                return m if par == 1 else None
            if m < BATCH // 2 - 1:
                return m if par == 1 else None
            return m if m == BATCH // 2 - 1 and par == 0 else None

        def uv_before(step, half):
            return (step - half * BATCH) * len(SEGS[half]) + SEG_TOTAL[half]

        @block.sync
        def _(sp):
            def load(n, slot, dst, src):
                if not isinstance(n, int) or n >= RAW:
                    sp.wait_ge(split_done, n - RAW + 1)
                sp.dma_start(dst, src).then_inc(raw_in[slot], 16)

            def load_item(item):
                n = index[item]
                kind = item[0]
                dst = raw_view(item)[0]
                if kind == "w":
                    src = (w_tiles0, w_tiles1)[item[1]][item[2], item[3], :, :]
                elif kind == "b":
                    c0 = (item[1] * BANKS + item[2]) * BANK
                    src = lora_b[:, c0:c0 + BANK]
                else:
                    src = x_pieces[(item[1] // PIECES) % BATCH, item[1] % PIECES, :, :]
                load(n, n % RAW, dst, src)

            def load_bias(half):
                c0 = half * BANKS * BANK
                sp.dma_start(bias_bc[:, :], b_base[c0:c0 + BANKS * BANK].partition_broadcast(P)).then_inc(bias_in, 16)

            def load_step(m, par, half):
                step = m * 2 + par
                b = step - half * BATCH
                static = isinstance(m, int)
                for i in range(PIECES):
                    if static:
                        piece = step * PIECES + i + AHEAD
                        if piece < NPIECES:
                            load_item(("x", piece))
                        for item in extras_after(step, i):
                            load_item(item)
                    else:
                        over = (i + AHEAD) // PIECES
                        slot = arrival_slot(i, half)
                        src = x_pieces[bass.ds(b + over, 1), (i + AHEAD) % PIECES, :, :]
                        load(arrival(step, i, half), slot, raw[:, slot, 0:PW], src.rearrange("a p n -> p (a n)"))
                    if static and step == BATCH and i == 4:
                        sp.wait_ge(res_biased, BATCH * BANKS)
                        load_bias(1)
                    if i == 1 and half == 0 and row_tile(m, par) is not None:
                        if not static or m >= 1:
                            sp.wait_ge(rows_summed, m)
                        sp.dma_start(rows[:, :], w_rows[bass.ds(m, 1), :, :].rearrange("a p n -> p (a n)")).then_inc(rows_in, 16)
                    if i == 3 and half == 1 and (not static or step - 1 >= BATCH):
                        sp.wait_ge(out_done, step * BANKS - BANKS)
                        sp.wait_ge(spilled, BATCH * 16)
                        pb = step - 1 - BATCH
                        sp.dma_start(hwt_hl[:, :, :].rearrange("p a n -> p (a n)").bitcast(F32),
                                     spill[bass.ds(pb, 1), :, :].rearrange("a p n -> p (a n)")).then_inc(hwt_loaded, 16)

            sp.dma_start(pack[:, :], cond_pack).then_inc(pack_in, 16)
            first = order[:index["x", PIECES + AHEAD]]
            for n, item in enumerate(first):
                load_item(item)
                if n == 2:
                    sp.dma_start(b2_bc[:, :], b2.partition_broadcast(BATCH)).then_inc(small_in, 16)
                    sp.dma_start(bk[:, :], bias_k).then_inc(small_in, 16)
                    sp.dma_start(brt_bc[:, :], b_router.partition_broadcast(P)).then_inc(small_in, 16)
                if n == len(first) - 1:
                    load_bias(0)
                if n == 12:
                    sp.dma_start(kern[:, :, :], weight).then_inc(kern_in, 16)
            load_step(0, 1, 0)
            with sp.Fori(*PAIRS) as k:
                load_step(k, 0, 0)
                load_step(k, 1, 0)
            load_step(BATCH // 2 - 1, 0, 0)
            load_step(BATCH // 2 - 1, 1, 0)
            load_step(BATCH // 2, 0, 1)
            load_step(BATCH // 2, 1, 1)
            with sp.Fori(*PAIRS) as k:
                load_step(k + BATCH // 2, 0, 1)
                load_step(k + BATCH // 2, 1, 1)
            load_step(BATCH - 1, 0, 1)
            load_step(BATCH - 1, 1, 1)
            load_step(BATCH, 0, 1)
            for q in range(2):
                for j in range(BANKS):
                    sp.wait_ge(stored[q][j], STEPS // 2 * 16)

        @block.gpsimd
        def _(pool):
            nc.gpsimd.memset(ident[:, :], 0.0).then_inc(const_step, 1)
            pool.wait_ge(const_step, 1)
            nc.gpsimd.affine_select(out=ident[:, :], in_=ident[:, :], compare_op=ALU.not_equal, fill=1.0,
                                    base=0, pattern=[[-1, P]], channel_multiplier=1).then_inc(consts, 1)
            nc.gpsimd.memset(ones_r[:, :].bitcast(F32), 1.0).then_inc(consts, 1)
            nc.gpsimd.memset(ranked[:, :, :], 0.0).then_inc(consts, 1)
            for e in range(EXP):
                nc.gpsimd.memset(inv_k[:, e:e + 1], 1.0 / (e + 1)).then_inc(consts, 1)

            def add_bias(pm, q):
                pool.wait_ge(res_in[q], pm * 16 + 16)
                for j in range(BANKS):
                    nc.gpsimd.tensor_tensor(out=res[:, q, j, :], in0=res[:, q, j, :],
                                            in1=bias_bc[:, j * BANK:(j + 1) * BANK], op=ALU.add).then_inc(res_biased, 1)

            for half in range(HALVES):
                pool.wait_ge(bias_in, 16 * half + 16)
                with pool.Fori(0, BATCH // 2) as k:
                    add_bias(k + half * (BATCH // 2), 0)
                    add_bias(k + half * (BATCH // 2), 1)

        @block.scalar
        def _(act):
            def hi_item(item):
                n = index[item]
                src, hi, _ = raw_view(item)
                act.wait_ge(raw_in[n % RAW], (n // RAW + 1) * 16)
                if item[0] == "x" and item[1] >= XSLOTS:
                    act.wait_ge(pieces_used, item[1] - XSLOTS + 1)
                if item[0] == "w" and item[1] == 1:
                    act.wait_ge(pieces_used, (BATCH - 1) * PIECES + item[2] // CPP + 1)
                if item[0] == "b" and item[1] == 1:
                    act.wait_ge(out_done, BATCH * BANKS)
                nc.scalar.activation(hi, src, ACT.Copy).then_inc(hi_done, 1)

            def load_rows(m, par, b, half):
                for j in range(BANKS):
                    if not isinstance(m, int) or m >= 1:
                        act.wait_ge(stored[par][j], m * 16)
                c0 = half * BANKS * BANK
                act.dma_start(res[:, par, :, :].rearrange("p a n -> p (a n)"),
                              x_rows[bass.ds(b, 1), :, c0:c0 + BANKS * BANK].rearrange("a p n -> p (a n)"))\
                   .then_inc(res_in[par], 16)

            def hi_step(m, par, half):
                static = isinstance(m, int)
                step = m * 2 + par
                q = (par + 1) % 2
                prev = step - 1
                phalf = prev // BATCH if static else half
                pb = prev % BATCH if static else prev - half * BATCH
                last = static and step == STEPS

                def store(j, q, pb, phalf, count):
                    act.wait_ge(final_done, count)
                    c0 = (phalf * BANKS + j) * BANK
                    act.dma_start(out[bass.ds(pb, 1), :, c0:c0 + BANK].rearrange("a p n -> p (a n)"), res[:, q, j, :])\
                       .then_inc(stored[q][j], 16)

                def extras(i):
                    if static:
                        for item in extras_after(step, i):
                            hi_item(item)

                for i in range(PIECES):
                    if i == 0:
                        act.wait_ge(pieces_used, step * PIECES)
                        if not static or prev >= 1:
                            act.wait_ge(out_done, prev * BANKS)
                        for s in reversed(range(len(SEGS[phalf]))):
                            a, z = SEGS[phalf][s]
                            nc.scalar.activation(uv_hi[:, a:z], ps_u[:, q, s, 0:z - a], ACT.Copy).then_inc(uhi_done, 1)
                        if static and step == 1:
                            act.wait_ge(wsum_done, 1)
                            nc.scalar.activation(wsum_bc[:, :], ps_o[:, :, :].rearrange("p a n -> p (a n)"), ACT.Copy)\
                              .then_inc(wsum_ready, 1)
                    if static:
                        piece = step * PIECES + i + AHEAD
                        if piece < NPIECES:
                            hi_item(("x", piece))
                    else:
                        slot = arrival_slot(i, half)
                        xs = (i + AHEAD) % XSLOTS
                        lap = (i + AHEAD + behind[half]) // RAW + 1
                        act.wait_ge(raw_in[slot], (step * (PIECES // RAW) + lap) * 16)
                        act.wait_ge(pieces_used, step * PIECES + (i + AHEAD - XSLOTS + 1))
                        nc.scalar.activation(x_hi[:, xs, :], raw[:, slot, 0:PW], ACT.Copy).then_inc(hi_done, 1)
                    if i == 1 and (not static or prev >= 1):
                        p2 = prev - 1
                        store(1, par, p2 % BATCH if static else p2 - half * BATCH, p2 // BATCH if static else half, prev * BANKS)
                    if i == 3 and phalf == 0:
                        act.wait_ge(hwt_done, prev + 1)
                        if not static or prev >= 1:
                            act.wait_ge(spilled, prev * 16)
                        nc.scalar.activation(hwt_hl[:, 0, :], ps_u[:, q, VBANK, HWT:HWT + P], ACT.Copy).then_inc(hwt_hi_done, 1)
                    if i == 2 and half == 0 and row_tile(m, par) is not None:
                        act.wait_ge(rows_in, (m + 1) * 16)
                        nc.scalar.activation(rows[:, :], rows[:, :], ACT.Copy, accum_out=row_sum[:, bass.ds(m, 1)])\
                          .then_inc(rows_summed, 1)
                    if i == 4 and not last:
                        load_rows(m, par, step % BATCH if static else step - half * BATCH, half)
                    if i == 2 and static and step == BATCH + 1:
                        act.wait_ge(wsum_done, 2)
                        act.wait_ge(final_done, BATCH * BANKS)
                        for j in range(BANKS):
                            nc.scalar.activation(wsum_bc[:, j * BANK:(j + 1) * BANK], ps_u[:, j, VBANK, :], ACT.Copy)\
                              .then_inc(wsum_ready, 1)
                    if i == 5 and phalf == 0:
                        act.wait_ge(hwt_split, prev + 1)
                        act.dma_start(spill[bass.ds(pb, 1), :, :].rearrange("a p n -> p (a n)"),
                                      hwt_hl[:, :, :].rearrange("p a n -> p (a n)").bitcast(F32)).then_inc(spilled, 16)
                    extras(i)
                    if i == 7:
                        store(0, q, pb, phalf, prev * BANKS + 1)
                        if last:
                            store(1, q, pb, phalf, prev * BANKS + 2)

            first = order[:index["x", PIECES + AHEAD]]
            for n, item in enumerate(first):
                if n < 2:
                    act.wait_ge(c_mm, n + 1)
                    nc.scalar.activation(hid[:, n, :], ps_u[:, 1, 0, 0:BATCH], ACT.Gelu,
                                         bias=pack[:, CP_B0 + n:CP_B0 + n + 1]).then_inc(c_act, 1)
                if n == 7:
                    act.wait_ge(c_dve, 1)
                    nc.scalar.activation(lg[:, :], lg[:, :], ACT.Exp).then_inc(c_act, 1)
                hi_item(item)
            load_rows(0, 0, 0, 0)
            hi_step(0, 1, 0)
            with act.Fori(*PAIRS) as k:
                hi_step(k, 0, 0)
                hi_step(k, 1, 0)
            hi_step(BATCH // 2 - 1, 0, 0)
            hi_step(BATCH // 2 - 1, 1, 0)
            hi_step(BATCH // 2, 0, 1)
            hi_step(BATCH // 2, 1, 1)
            with act.Fori(*PAIRS) as k:
                hi_step(k + BATCH // 2, 0, 1)
                hi_step(k + BATCH // 2, 1, 1)
            hi_step(BATCH - 1, 0, 1)
            hi_step(BATCH - 1, 1, 1)
            hi_step(BATCH, 0, 1)

        @block.vector
        def _(dve):
            def minus(out, a, hi):
                return nc.vector.tensor_tensor(out=out, in0=a, in1=hi.bitcast(F32), op=ALU.subtract)

            def lo_item(item):
                n = index[item]
                src, hi, lo = raw_view(item)
                dve.wait_ge(hi_done, n + 1)
                minus(lo, src, hi).then_inc(split_done, 1)

            def mix_kernels(step, b, par, static):
                base = step * MIX_STEPS
                if not static or step >= 2:
                    dve.wait_ge(out_done, (step - 1) * BANKS)
                for k in range(KERN):
                    coef = att_bc[:, bass.ds(b * KERN + k, 1)]
                    if k == 0:
                        nc.vector.tensor_scalar(mix[:, :], kern[:, k, :], coef, None, ALU.mult).then_inc(mix_step, 1)
                    else:
                        nc.vector.scalar_tensor_tensor(out=mix[:, :], in0=kern[:, k, :], scalar=coef, in1=mix[:, :],
                                                       op0=ALU.mult, op1=ALU.add).then_inc(mix_step, 1)
                    dve.wait_ge(mix_step, base + (k + 1))
                nc.vector.tensor_copy(mix_hi[:, par, :], mix[:, :]).then_inc(mix_step, 1)
                dve.wait_ge(mix_step, base + MIX_STEPS)
                minus(mix_lo[:, par, :], mix[:, :], mix_hi[:, par, :]).then_inc(mix_split, 1)

            def route(prev, pb, q):
                base = prev * ROUTE_STEPS
                stage = [0]

                def then(ins):
                    stage[0] += 1
                    ins.then_inc(route_step, 1)
                    dve.wait_ge(route_step, base + stage[0])

                dve.wait_ge(vmix_done, prev + 1)
                def mixed(cols):
                    return nc.vector.scalar_tensor_tensor(
                        out=low[:, cols], in0=rt_sum[:, cols], scalar=mixb[:, bass.ds(pb, 1)],
                        in1=ps_u[:, q, VBANK, cols], op0=ALU.mult, op1=ALU.add)

                logits = low[:, ER:RT]
                then(mixed(slice(ER, RT)))
                then(nc.vector.tensor_tensor(out=logits, in0=logits, in1=brt_bc[:, :], op=ALU.add))
                stage[0] += 1
                mixed(slice(0, ER)).then_inc(route_step, 1)
                dve.wait_ge(consts, 3 + EXP)
                then(nc.vector.max(ranked[:, 0, EXP:2 * EXP], logits))
                for s, (a, o) in zip((1, 2, 4), ((0, 1), (1, 2), (2, 0))):
                    dst = taus[:, :] if s == 4 else ranked[:, o, EXP:2 * EXP]
                    then(nc.vector.tensor_tensor(out=dst, in0=ranked[:, a, EXP:2 * EXP],
                                                 in1=ranked[:, a, EXP - s:2 * EXP - s], op=ALU.add))
                then(nc.vector.scalar_tensor_tensor(out=taus[:, :], in0=taus[:, :], scalar=-1.0, in1=inv_k[:, :],
                                                    op0=ALU.add, op1=ALU.mult))
                then(nc.vector.reduce_max(tau[:, :], taus[:, :], AX.X))
                then(nc.vector.tensor_scalar(wts[:, :], logits, tau[:, 0:1], 0.0, ALU.subtract, ALU.max))
                nc.vector.tensor_tensor(out=hw[:, :].rearrange("p (e r) -> p e r", r=RANK),
                                        in0=low[:, 0:ER].rearrange("p (e r) -> p e r", r=RANK),
                                        in1=wts[:, :].unsqueeze(2).broadcast_to([P, EXP, RANK]), op=ALU.mult)\
                  .then_inc(hw_ready, 1)

            def split_uv(s, q, prev, phalf):
                segs = SEGS[phalf]
                dve.wait_ge(uhi_done, uv_before(prev, phalf) + (len(segs) - s))
                a, z = segs[s]
                minus(uv_lo[:, a:z], ps_u[:, q, s, 0:z - a], uv_hi[:, a:z]).then_inc(u_split, 1)

            def finish(j, q, prev, pb):
                dve.wait_ge(out_done, prev * BANKS + j + 1)
                nc.vector.scalar_tensor_tensor(out=ps_o[:, j, :], in0=wsum_bc[:, j * BANK:(j + 1) * BANK],
                                               scalar=mixb[:, bass.ds(pb, 1)], in1=ps_o[:, j, :],
                                               op0=ALU.mult, op1=ALU.add).then_inc(fin_step, 1)
                dve.wait_ge(fin_step, prev * BANKS + j + 1)
                dve.wait_ge(res_biased, prev * BANKS + j + 1)
                nc.vector.tensor_tensor(out=res[:, q, j, :], in0=res[:, q, j, :], in1=ps_o[:, j, :], op=ALU.add)\
                  .then_inc(final_done, 1)

            def lo_step(m, par, half):
                static = isinstance(m, int)
                step = m * 2 + par
                q = (par + 1) % 2
                prev = step - 1
                phalf = prev // BATCH if static else half
                pb = prev % BATCH if static else prev - half * BATCH

                def extras(i):
                    if static:
                        for item in extras_after(step, i):
                            lo_item(item)

                for i in range(PIECES):
                    if i == 0:
                        for s in reversed(range(len(SEGS[phalf]))):
                            split_uv(s, q, prev, phalf)
                    if static:
                        piece = step * PIECES + i + AHEAD
                        if piece < NPIECES:
                            lo_item(("x", piece))
                    else:
                        slot = arrival_slot(i, half)
                        xs = (i + AHEAD) % XSLOTS
                        dve.wait_ge(hi_done, step * PIECES + (i + AHEAD + behind[half] + 1))
                        minus(x_lo[:, xs, :], raw[:, slot, 0:PW], x_hi[:, xs, :]).then_inc(split_done, 1)
                    if i == 1 and phalf == 0:
                        route(prev, pb, q)
                    if i == 6 and static and step == BATCH:
                        dve.wait_ge(rows_summed, ROW_TILES)
                        parts = row_sum[:, :].rearrange("p (n a) -> p n a", a=2)
                        nc.vector.tensor_tensor(out=tots[:, :], in0=parts[:, :, 0], in1=parts[:, :, 1], op=ALU.add)\
                          .then_inc(rows_step, 1)
                        dve.wait_ge(rows_step, 1)
                        nc.vector.tensor_tensor(out=rows[:, :].rearrange("p (n o) -> p n o", o=P),
                                                in0=ident[:, :].unsqueeze(1).broadcast_to([P, ROW_TILES // 2, P]),
                                                in1=tots[:, :].unsqueeze(2).broadcast_to([P, ROW_TILES // 2, P]),
                                                op=ALU.mult).then_inc(rows_step, 1)
                    if i == 2 and not (static and step == STEPS):
                        mix_kernels(step, step % BATCH if static else step - half * BATCH, par, static)
                    if i == 3 and phalf == 0:
                        dve.wait_ge(hwt_hi_done, prev + 1)
                        minus(hwt_hl[:, 1, :], ps_u[:, q, VBANK, HWT:HWT + P], hwt_hl[:, 0, :]).then_inc(hwt_split, 1)
                    extras(i)
                    if i == 5:
                        if static and step == 1:
                            dve.wait_ge(wsum_ready, 1)
                        if static and step == BATCH + 1:
                            dve.wait_ge(wsum_ready, 1 + BANKS)
                        finish(0, q, prev, pb)
                    if i == 7:
                        finish(1, q, prev, pb)

            def attention(n):
                if n == 4:
                    dve.wait_ge(c_mm, 3)
                    dve.wait_ge(small_in, 48)
                    nc.vector.tensor_tensor(out=lg[:, :], in0=ps_u[0:BATCH, 1, 0, 0:KERN], in1=b2_bc[:, :], op=ALU.add)\
                      .then_inc(c_step, 1)
                    dve.wait_ge(c_step, 1)
                    nc.vector.reduce_max(lgs[:, 0:1], lg[:, :], AX.X).then_inc(c_step, 1)
                    dve.wait_ge(c_step, 2)
                    nc.vector.tensor_scalar(lg[:, :], lg[:, :], lgs[:, 0:1], None, ALU.subtract).then_inc(c_dve, 1)
                if n == 8:
                    dve.wait_ge(c_act, 3)
                    nc.vector.reduce_sum(lgs[:, 0:1], lg[:, :], AX.X).then_inc(c_step, 1)
                    dve.wait_ge(c_step, 3)
                    nc.vector.reciprocal(lgs[:, 1:2], lgs[:, 0:1]).then_inc(c_step, 1)
                    dve.wait_ge(c_step, 4)
                    nc.vector.tensor_scalar(lg[:, :], lg[:, :], lgs[:, 1:2], None, ALU.mult).then_inc(c_dve, 1)
                if n == 16:
                    dve.wait_ge(c_mm, 4)
                    nc.vector.tensor_copy(att_t[:, :], ps_u[0:KERN, 1, 0, 0:BATCH]).then_inc(c_step, 1)
                    dve.wait_ge(c_step, 5)
                    nc.vector.tensor_tensor(out=att_d[:, :, :], in0=att_t[:, :].unsqueeze(2).broadcast_to([KERN, BATCH, KERN]),
                                            in1=ident[0:KERN, 0:KERN].unsqueeze(1).broadcast_to([KERN, BATCH, KERN]),
                                            op=ALU.mult).then_inc(c_dve, 1)
                if n == 26:
                    dve.wait_ge(c_mm, 5)
                    nc.vector.tensor_copy(att_bc[:, :], ps_u[:, 1, 0, 0:BATCH * KERN]).then_inc(c_step, 1)
                    nc.vector.tensor_copy(mixb[:, :], ps_u[:, 1, 1, 0:BATCH]).then_inc(c_dve, 1)
                if n == index["w", 0, CHUNKS - 1, TILES - 1]:
                    dve.wait_ge(c_step, 6)
                    dve.wait_ge(c_dve, 4)
                    dve.wait_ge(kern_in, 16)
                    mix_kernels(0, 0, 0, True)

            first = order[:index["x", PIECES + AHEAD]]
            for n, item in enumerate(first):
                lo_item(item)
                attention(n)
            dve.wait_ge(wsum_done, 1)
            nc.vector.tensor_copy(rt_sum[:, :], ps_u[:, 1, VBANK, 0:RT]).then_inc(rtsum_ready, 1)
            dve.wait_ge(rtsum_ready, 1)
            lo_step(0, 1, 0)
            with dve.Fori(*PAIRS) as k:
                lo_step(k, 0, 0)
                lo_step(k, 1, 0)
            lo_step(BATCH // 2 - 1, 0, 0)
            lo_step(BATCH // 2 - 1, 1, 0)
            lo_step(BATCH // 2, 0, 1)
            lo_step(BATCH // 2, 1, 1)
            with dve.Fori(*PAIRS) as k:
                lo_step(k + BATCH // 2, 0, 1)
                lo_step(k + BATCH // 2, 1, 1)
            lo_step(BATCH - 1, 0, 1)
            lo_step(BATCH - 1, 1, 1)
            lo_step(BATCH, 0, 1)

        @block.tensor
        def _(pe):
            mm = nc.tensor.matmul

            def chunk(c, par, half):
                xs, xc = (c // CPP) % XSLOTS, slice(c % CPP * CH, (c % CPP + 1) * CH)
                hi, lo = x_hi[:, xs, xc], x_lo[:, xs, xc]
                first, last = c == 0, c == CHUNKS - 1
                for n, (a_part, w_part) in enumerate(((hi, w_hi), (hi, w_lo), (lo, w_hi))):
                    for s, (a, z) in enumerate(SEGS[half]):
                        ins = mm(ps_u[:, par, s, 0:z - a], a_part, w_part[:, c, a:z],
                                 start=first and n == 0, stop=last and n == 2)
                return ins

            def split_product(dst, a_hi, a_lo, b_hi_, b_lo_, start, stop):
                mm(dst, a_hi, b_hi_, start=start, stop=False)
                mm(dst, a_hi, b_lo_, start=False, stop=False)
                return mm(dst, a_lo, b_hi_, start=False, stop=stop)

            def col_sums(dst, c, a, z):
                mm(dst, ones_r[:, :], w_hi[:, c, a:z], start=(c == 0), stop=False)
                return mm(dst, ones_r[:, :], w_lo[:, c, a:z], start=False, stop=(c == CHUNKS - 1))

            def out_bank(j, m, par, static, step, phalf):
                q = (par + 1) % 2
                prev = step - 1
                cols = slice(j * BANK, (j + 1) * BANK)
                if j == 0:
                    pe.wait_ge(u_split, uv_before(prev, phalf) + len(SEGS[phalf]))
                if not static or prev >= 1:
                    pe.wait_ge(final_done, (prev - 1) * BANKS + j + 1)
                if static and prev == 0 and j == 0:
                    pe.wait_ge(wsum_ready, 1)
                if j == 0:
                    pe.wait_ge(mix_split, prev + 1)
                    if phalf == 0:
                        pe.wait_ge(hwt_split, prev + 1)
                    else:
                        pe.wait_ge(hwt_loaded, (prev - BATCH + 1) * 16)
                if static and prev % BATCH == 0:
                    pe.wait_ge(split_done, index["b", prev // BATCH, j] + 1)
                split_product(ps_o[:, j, :], mix_hi[:, q, :], mix_lo[:, q, :], uv_hi[:, cols], uv_lo[:, cols], True, False)
                split_product(ps_o[:, j, :], hwt_hl[:, 0, :], hwt_hl[:, 1, :], b_hi[:, cols], b_lo[:, cols],
                              False, True).then_inc(out_done, 1)

            def mm_step(m, par, half):
                static = isinstance(m, int)
                step = m * 2 + par
                q = (par + 1) % 2
                prev = step - 1
                phalf = prev // BATCH if static else half
                has_prev = not static or step > 0
                has_base = not static or step < STEPS
                for i in range(PIECES):
                    if has_base:
                        if static:
                            pe.wait_ge(split_done, index["x", step * PIECES + i] + 1)
                        else:
                            pe.wait_ge(split_done, step * PIECES + (i + behind[half] + 1))
                        for c in range(i * CPP, i * CPP + CPP):
                            if static and step % BATCH == 0:
                                pe.wait_ge(split_done, index["w", half, c, TILES - 1] + 1)
                            ins = chunk(c, par, half)
                            if static and step == 0:
                                for j in range(BANKS):
                                    col_sums(ps_o[:, j, :], c, j * BANK, (j + 1) * BANK)
                                ins2 = col_sums(ps_u[:, 1, VBANK, 0:RT], c, VCOL, WR)
                                if c == CHUNKS - 1:
                                    ins2.then_inc(wsum_done, 1)
                        ins.then_inc(pieces_used, 1)
                    if static and step == BATCH + 1 and i == 0:
                        pe.wait_ge(rows_step, 2)
                        for j in range(BANKS):
                            ins2 = mm(ps_u[:, j, VBANK, :], ones_r[:, :].bitcast(F32), rows[:, j * BANK:(j + 1) * BANK],
                                      start=True, stop=True)
                        ins2.then_inc(wsum_done, 1)
                    if static and step == 0:
                        attention(i)
                    if not has_prev:
                        continue
                    if i == 0 and phalf == 0:
                        pe.wait_ge(u_split, uv_before(prev, 0) + 1)
                        pe.wait_ge(mix_split, prev + 1)
                        split_product(ps_u[:, q, VBANK, 0:RT], mix_hi[:, q, :], mix_lo[:, q, :],
                                      uv_hi[:, VCOL:WR], uv_lo[:, VCOL:WR], True, True).then_inc(vmix_done, 1)
                    if i == 2 and phalf == 0:
                        pe.wait_ge(hw_ready, prev + 1)
                        nc.tensor.transpose(ps_u[:, q, VBANK, HWT:HWT + P], hw[:, :], ident[:, :]).then_inc(hwt_done, 1)
                    if i == 4:
                        out_bank(0, m, par, static, step, phalf)
                    if i == 6:
                        out_bank(1, m, par, static, step, phalf)

            small = ps_u[:, 1, 0, :]

            def attention(i):
                if i == 1:
                    pe.wait_ge(c_dve, 2)
                    nc.tensor.transpose(small[0:KERN, 0:BATCH], lg[:, :], ident[0:BATCH, 0:BATCH]).then_inc(c_mm, 1)
                if i == 3:
                    pe.wait_ge(c_dve, 3)
                    mm(ps_u[:, 1, 1, 0:BATCH], bk[:, :], att_t[:, :], start=True, stop=True)
                    mm(small[:, 0:BATCH * KERN], ones_r[0:KERN, :].bitcast(F32), att_d[:, :, :].rearrange("k b n -> k (b n)"),
                       start=True, stop=True).then_inc(c_mm, 1)

            pe.wait_ge(pack_in, 16)
            mm(small[:, 0:BATCH], pack[:, CP_W0:CP_W1], pack[:, 0:BATCH], start=True, stop=True).then_inc(c_mm, 1)
            pe.wait_ge(c_act, 1)
            mm(small[:, 0:BATCH], pack[:, CP_W1:CP_W2], hid[:, 0, :], start=True, stop=True).then_inc(c_mm, 1)
            pe.wait_ge(c_act, 2)
            mm(small[0:BATCH, 0:KERN], hid[:, 1, :], pack[:, CP_W2:CP_B0], start=True, stop=True).then_inc(c_mm, 1)
            pe.wait_ge(consts, 3 + EXP)
            mm_step(0, 0, 0)
            pe.wait_ge(c_dve, 4)
            pe.wait_ge(c_step, 6)
            pe.wait_ge(rtsum_ready, 1)
            mm_step(0, 1, 0)
            with pe.Fori(*PAIRS) as k:
                mm_step(k, 0, 0)
                mm_step(k, 1, 0)
            mm_step(BATCH // 2 - 1, 0, 0)
            mm_step(BATCH // 2 - 1, 1, 0)
            mm_step(BATCH // 2, 0, 1)
            mm_step(BATCH // 2, 1, 1)
            with pe.Fori(*PAIRS) as k:
                mm_step(k + BATCH // 2, 0, 1)
                mm_step(k + BATCH // 2, 1, 1)
            mm_step(BATCH - 1, 0, 1)
            mm_step(BATCH - 1, 1, 1)
            mm_step(BATCH, 0, 1)


def kernel(**inputs):
    import numpy as np
    import concourse.bacc as bacc
    from concourse.bass_utils import run_bass_kernel_spmd

    a = {k: np.asarray(v) for k, v in inputs.items()}
    x = a["x"]
    low = np.concatenate([a["L0_ffn_lora_A"].transpose(1, 0, 2).reshape(HID, ER), a["L0_ffn_W_router"].T], axis=1)
    w_t = a["L0_ffn_W_base"].T

    def tiled(m):
        return m.reshape(CHUNKS, P, TILES, -1).transpose(0, 2, 1, 3)

    laid = {
        "x_pieces": x.reshape(BATCH, CH, PIECES, CPP, P).transpose(0, 2, 4, 3, 1).reshape(BATCH, PIECES, P, PW),
        "x_rows": x,
        "w_tiles0": tiled(np.concatenate([w_t[:, :DOUT // 2], low], axis=1)),
        "w_tiles1": tiled(w_t[:, DOUT // 2:]),
        "w_rows": a["L0_ffn_W_base"][DOUT // 2:].reshape(-1, P, HID // ROW_W, ROW_W).transpose(0, 2, 1, 3).reshape(ROW_TILES, P, ROW_W),
        "lora_b": a["L0_ffn_lora_B"].reshape(ER, DOUT),
        "b_base": a["L0_ffn_b_base"],
        "b_router": a["L0_ffn_b_router"],
        "weight": a["L0_cond_weight"][..., 0].transpose(2, 0, 1),
        "bias_k": a["L0_cond_bias_k"],
        "b2": a["L0_cond_b2"],
        "cond_pack": np.concatenate([a["cond_128"].T, a["L0_cond_W0"], a["L0_cond_W1"], a["L0_cond_W2"],
                                     a["L0_cond_b0"][:, None], a["L0_cond_b1"][:, None]], axis=1),
    }
    nc = bacc.Bacc("TRN2", target_bir_lowering=False, num_devices=1,
                   dynamic_dma_scratch_size=1024)
    arrays, args = {}, []
    for name, v in laid.items():
        v = np.ascontiguousarray(v)
        arrays[f"in_{name}"] = v
        args.append(nc.dram_tensor(f"in_{name}", v.shape, mybir.dt.from_np(v.dtype), kind="ExternalInput").ap())
    args.append(nc.dram_tensor("out_0", (BATCH, CH, DOUT), F32, kind="ExternalOutput").ap())
    args.append(nc.dram_tensor("hwt_spill", (BATCH, P, 2 * P), F32, kind="Internal").ap())
    build(nc, *args)
    r = run_bass_kernel_spmd(nc, [arrays], core_ids=[0])
    return r.results[0]["out_0"]
```
